# Optimizing a Trainium2 kernel written in Bass

```python
import numpy as np
import jax
import jax.numpy as jnp

def _softmax(x, axis=-1):
    return jax.nn.softmax(x, axis=axis)

def _gelu(x):
    return jax.nn.gelu(x, approximate=True)

def _silu(x):
    return jax.nn.silu(x)

def _sigmoid(x):
    return jax.nn.sigmoid(x)

def _layernorm(x, axis=-1, eps=1e-05):
    m = jnp.mean(x, axis=axis, keepdims=True)
    v = jnp.var(x, axis=axis, keepdims=True)
    return (x - m) / jnp.sqrt(v + eps)

def _scatter_add(tgt, idx, src, axis=0):
    return tgt.at[idx].add(src)

def _segment_sum(src, seg, n):
    return jax.ops.segment_sum(src, seg, n)
kernel_name = 'mk_adj_resnorm_d1_adj_r2_dffa20'

def setup_inputs(seed: int=0):
    np.random.seed(seed)
    _w = jnp.asarray

    def _rec_inputs():
        import jax
        import jax.numpy as jnp
        _gk = jax.random.key(seed)
        x = -0.0002928 + 1 * jax.random.normal(jax.random.fold_in(_gk, 1), (8192, 128), jnp.float32)
        _w = (1.0 + jnp.arange(8192, dtype=jnp.float32)) ** (-0.5)
        _w = _w / _w.mean()
        _pij = jnp.clip(0.000976562 * _w[:, None] * _w[None, :], 0.0, 1.0)
        _a = jax.random.uniform(jax.random.fold_in(_gk, 2), (8192, 8192)) < _pij
        _a = jnp.logical_or(_a, jnp.eye(8192, dtype=bool))
        _af = _a.astype(jnp.float32)
        _af = _af * jax.random.uniform(jax.random.fold_in(_gk, 3), (8192, 8192), jnp.float32, 0.05, 6.10351e-05)
        adj = _af
        return (x, adj)
    x, adj = _rec_inputs()

    def _L0_gnn_setup():
        import jax, jax.numpy as jnp
        import numpy as np
        N_NODES = 8192
        D_FEAT = 128
        key = jax.random.key(seed)
        k1, k2, k3, k4 = jax.random.split(key, 4)
        X = jax.random.normal(k1, (N_NODES, D_FEAT), dtype=jnp.float32)
        A_hat = jax.random.uniform(k2, (N_NODES, N_NODES), dtype=jnp.float32) / N_NODES
        w = jax.random.uniform(k3, (N_NODES,), dtype=jnp.float32)
        W_agg = jax.random.normal(k4, (D_FEAT, D_FEAT), dtype=jnp.float32) / np.sqrt(D_FEAT)
        return {'X': X, 'A_hat': A_hat, 'w': w, 'W_agg': W_agg}
    _L0_gnn_all = _L0_gnn_setup()
    _L0_gnn_in = {k: v for k, v in _L0_gnn_all.items() if k in ('w', 'W_agg')}
    del _L0_gnn_all
    return {'x': x, 'adj': adj, 'L0_gnn_w': _L0_gnn_in['w'], 'L0_gnn_W_agg': _L0_gnn_in['W_agg']}

def reference(x, adj, L0_gnn_w, L0_gnn_W_agg):
    import jax
    import jax.numpy as jnp

    def _L0_gnn_ref(X, A_hat, w, W_agg):
        import jax, jax.numpy as jnp
        import numpy as np
        N_NODES = 8192
        D_FEAT = 128
        agg = jnp.matmul(jnp.matmul(A_hat, X), W_agg)
        agg = jax.nn.relu(agg)
        s = jax.nn.sigmoid(w)[:, None]
        return s * agg + (1.0 - s) * X
    x = _layernorm(x + _L0_gnn_ref(x, adj, L0_gnn_w, L0_gnn_W_agg), axis=-1)
    return x

_drawn_inputs = setup_inputs


def setup_inputs(seed=0):
    import zlib

    import numpy as np

    out = dict(_drawn_inputs(seed))
    spreads = {}
    factors = {}
    for name, (base, spread) in spreads.items():
        noise = np.random.default_rng([zlib.crc32(name.encode()), seed]).standard_normal(out[name].shape)
        drawn = base * np.exp(spread * noise) if base else spread * noise
        out[name] = jnp.asarray(drawn.astype(out[name].dtype))
    for name, factor in factors.items():
        out[name] = (out[name] * factor).astype(out[name].dtype)
    return out
```

```python
from contextlib import ExitStack

import concourse.bass as bass
from concourse import mybir

F32 = mybir.dt.float32
F32R = mybir.dt.float32r
ALU = mybir.AluOpType
ACT = mybir.ActivationFunctionType

P = 128
NODES = 8192
D = 128
EPS = 1e-5

BLOCK = 1024
BLOCKS = NODES // BLOCK
TILES = BLOCK // P
BANK = 512
HALVES = BLOCK // BANK

CHUNKS = NODES // P
GROUP_CHUNKS = 2
GROUP = GROUP_CHUNKS * BLOCK
GROUPS = CHUNKS // GROUP_CHUNKS
RING = 4
ROUNDS = GROUPS // RING

X_PIECES = 4
X_CHUNKS = CHUNKS // X_PIECES
X_PIECE = X_CHUNKS * D
X_RING = 2
X_LOAD_AT = [0, 2, 6, 14]
X_SPLIT_AT = [0, 4, 12, 20]


def build(nc, adj_groups, x_chunks, x_rows, gate_w, w_agg, out_rows):
    with ExitStack() as ctx:
        def sbuf(name, shape, dtype=F32):
            return ctx.enter_context(nc.sbuf_tensor(name, shape, dtype))

        def psum(name, shape):
            return ctx.enter_context(nc.psum_tensor(name, shape, F32))

        def semaphore(name):
            return ctx.enter_context(nc.semaphore(name))

        adj_raw = sbuf("adj_raw", [P, RING, GROUP])
        adj_high = sbuf("adj_high", [P, RING, GROUP], F32R)
        adj_low = sbuf("adj_low", [P, RING, GROUP], F32R)
        x_raw = sbuf("x_raw", [P, X_RING, X_PIECE])
        x_high = sbuf("x_high", [P, CHUNKS * D], F32R)
        x_low = sbuf("x_low", [P, CHUNKS * D], F32R)
        weights = sbuf("weights", [D, D])
        gate_logits = sbuf("gate_logits", [P, BLOCKS, TILES])
        gate = sbuf("gate", [P, BLOCKS, TILES])
        keep = sbuf("keep", [P, BLOCKS, TILES])
        y_t = sbuf("y_t", [D, TILES, P])
        rows = sbuf("rows", [P, TILES, D])
        gated = sbuf("gated", [P, TILES, D])
        mixed = sbuf("mixed", [P, TILES, D])
        normed = sbuf("normed", [P, TILES, D])
        stats = sbuf("stats", [P, TILES, 6])
        mean_sum = sbuf("mean_sum", [P, TILES])
        mean_gap = sbuf("mean_gap", [P, TILES])
        square_gap = sbuf("square_gap", [P, TILES])
        deviation = sbuf("deviation", [P, TILES])
        variance = sbuf("variance", [P, TILES])
        eps = sbuf("eps", [P, 1])
        std = sbuf("std", [P, TILES])
        var_eps = sbuf("var_eps", [P, TILES])
        guess = sbuf("guess", [P, TILES])
        square = sbuf("square", [P, TILES])
        factor = sbuf("factor", [P, TILES])
        rstd = sbuf("rstd", [P, TILES])
        shift = sbuf("shift", [P, TILES])

        y_acc = psum("y_acc", [D, 2, HALVES, BANK])
        agg = psum("agg", [P, TILES, D])

        adj_landed = [semaphore(f"adj_landed{s}") for s in range(RING)]
        x_landed = [semaphore(f"x_landed{s}") for s in range(X_RING)]
        x_high_ready = semaphore("x_high_ready")
        x_low_ready = semaphore("x_low_ready")
        high_ready = semaphore("high_ready")
        low_ready = semaphore("low_ready")
        group_used = semaphore("group_used")
        y_copied = semaphore("y_copied")
        agg_ready = semaphore("agg_ready")
        gated_ready = semaphore("gated_ready")
        mixed_ready = semaphore("mixed_ready")
        stats_ready = semaphore("stats_ready")
        merge_step = semaphore("merge_step")
        variance_ready = semaphore("variance_ready")
        std_ready = semaphore("std_ready")
        rstd_step = semaphore("rstd_step")
        rstd_ready = semaphore("rstd_ready")
        normed_ready = semaphore("normed_ready")
        weights_landed = semaphore("weights_landed")
        logits_landed = semaphore("logits_landed")
        rows_landed = semaphore("rows_landed")
        gate_ready = semaphore("gate_ready")
        keep_ready = semaphore("keep_ready")
        eps_ready = semaphore("eps_ready")
        out_stored = semaphore("out_stored")

        block = ctx.enter_context(nc.Block())

        @block.sync
        def _(sp):
            def load_group(round_, slot, first_round):
                if not first_round:
                    sp.wait_ge(low_ready, RING * (round_ - 1) + slot + 1)
                sp.dma_start(adj_raw[:, slot, :], adj_groups[round_ * RING + slot])\
                  .then_inc(adj_landed[slot], 16)

            for r in range(ROUNDS):
                for s in range(RING):
                    if r * RING + s in X_LOAD_AT:
                        piece = X_LOAD_AT.index(r * RING + s)
                        if piece >= X_RING:
                            sp.wait_ge(x_low_ready, piece - X_RING + 1)
                        sp.dma_start(x_raw[:, piece % X_RING, :],
                                     x_chunks[:, piece * X_PIECE:(piece + 1) * X_PIECE])\
                          .then_inc(x_landed[piece % X_RING], 16)
                    load_group(r, s, r == 0)
            with sp.Fori(ROUNDS, BLOCKS * ROUNDS) as r:
                for s in range(RING):
                    load_group(r, s, False)

        @block.gpsimd
        def _(pool):
            pool.dma_start(gate_logits[:, :, :], gate_w).then_inc(logits_landed, 16)
            pool.dma_start(weights[:, :], w_agg).then_inc(weights_landed, 16)
            pool.dma_start(rows[:, :, :], x_rows[0]).then_inc(rows_landed, 16)

            def store(b):
                pool.wait_ge(normed_ready, b + 1)
                pool.dma_start(out_rows[b], normed[:, :, :]).then_inc(out_stored, 16)

            with pool.Fori(0, BLOCKS - 1) as b:
                pool.wait_ge(mixed_ready, b + 1)
                pool.dma_start(rows[:, :, :], x_rows[b + 1]).then_inc(rows_landed, 16)
                store(b)
            store(BLOCKS - 1)
            pool.wait_ge(out_stored, 16 * BLOCKS)

        @block.scalar
        def _(act):
            def split_high(round_, slot, first_round):
                act.wait_ge(adj_landed[slot], 16 * (round_ + 1))
                if not first_round:
                    act.wait_ge(group_used, RING * (round_ - 1) + slot + 1)
                nc.scalar.activation(adj_high[:, slot, :], adj_raw[:, slot, :], ACT.Copy)\
                  .then_inc(high_ready, 1)

            def split_x_high(piece):
                act.wait_ge(x_landed[piece % X_RING], 16 * (piece // X_RING + 1))
                nc.scalar.activation(x_high[:, piece * X_PIECE:(piece + 1) * X_PIECE],
                                     x_raw[:, piece % X_RING, :], ACT.Copy)\
                  .then_inc(x_high_ready, 1)

            def stream(first, end):
                with act.Fori(first, end) as r:
                    for s in range(RING):
                        split_high(r, s, False)

            def copy_y(b, parity):
                act.wait_ge(group_used, GROUPS * (b + 1))
                nc.scalar.activation(y_t[:, :, :].rearrange("d t p -> d (t p)"),
                                     y_acc[:, parity, :, :].rearrange("d h n -> d (h n)"),
                                     ACT.Copy).then_inc(y_copied, 1)

            def gate_agg(b, first_block):
                act.wait_ge(agg_ready, b + 1)
                if not first_block:
                    act.wait_ge(mixed_ready, b)
                for t in range(TILES):
                    last = nc.scalar.activation(gated[:, t, :], agg[:, t, :], ACT.Relu,
                                                scale=gate_of(b, t))
                last.then_inc(gated_ready, 1)

            def gate_of(b, t):
                return gate[:, b, t:t + 1]

            def root(b):
                act.wait_ge(variance_ready, b + 1)
                nc.scalar.activation(std[:, :], variance[:, :], ACT.Sqrt, bias=eps[:, 0:1])\
                  .then_inc(std_ready, 1)

            def normalize(b, first_block):
                act.wait_ge(rstd_ready, b + 1)
                if not first_block:
                    act.wait_ge(out_stored, 16 * b)
                for t in range(TILES):
                    last = nc.scalar.activation(normed[:, t, :], mixed[:, t, :], ACT.Identity,
                                                scale=rstd[:, t:t + 1], bias=shift[:, t:t + 1])
                last.then_inc(normed_ready, 1)

            act.wait_ge(logits_landed, 16)
            nc.scalar.activation(gate[:, :, :], gate_logits[:, :, :], ACT.Sigmoid)\
              .then_inc(gate_ready, 1)
            for r in range(ROUNDS):
                for s in range(RING):
                    if r * RING + s in X_SPLIT_AT:
                        split_x_high(X_SPLIT_AT.index(r * RING + s))
                    split_high(r, s, r == 0)
            act.wait_ge(eps_ready, 1)
            act.wait_ge(gate_ready, 1)

            def stream_block(b, parity, first_block):
                r0 = b * ROUNDS
                stream(r0, r0 + 1)
                copy_y(b - 1, parity)
                stream(r0 + 1, r0 + 3)
                gate_agg(b - 1, first_block)
                stream(r0 + 3, r0 + 5)
                root(b - 1)
                stream(r0 + 5, r0 + 7)
                normalize(b - 1, first_block)
                stream(r0 + 7, r0 + 8)

            stream_block(1, 0, True)
            with act.Fori(1, BLOCKS // 2) as pair:
                stream_block(2 * pair, 1, False)
                stream_block(2 * pair + 1, 0, False)
            copy_y(BLOCKS - 1, 1)
            gate_agg(BLOCKS - 1, False)
            root(BLOCKS - 1)
            normalize(BLOCKS - 1, False)

        @block.vector
        def _(dve):
            def split_low(round_, slot):
                dve.wait_ge(high_ready, RING * round_ + slot + 1)
                nc.vector.tensor_tensor(adj_low[:, slot, :], adj_raw[:, slot, :],
                                        adj_high[:, slot, :].bitcast(F32), ALU.subtract)\
                  .then_inc(low_ready, 1)

            def split_x_low(piece):
                dve.wait_ge(x_high_ready, piece + 1)
                part = slice(piece * X_PIECE, (piece + 1) * X_PIECE)
                nc.vector.tensor_tensor(x_low[:, part], x_raw[:, piece % X_RING, :],
                                        x_high[:, part].bitcast(F32), ALU.subtract)\
                  .then_inc(x_low_ready, 1)

            def stream(first, end):
                with dve.Fori(first, end) as r:
                    for s in range(RING):
                        split_low(r, s)

            def mix(b, first_block):
                dve.wait_ge(gated_ready, b + 1)
                dve.wait_ge(rows_landed, 16 * (b + 1))
                if not first_block:
                    dve.wait_ge(normed_ready, b)
                for t in range(TILES):
                    last = nc.vector.scalar_tensor_tensor(mixed[:, t, :], rows[:, t, :],
                                                          keep[:, b, t:t + 1], gated[:, t, :],
                                                          ALU.mult, ALU.add)
                last.then_inc(mixed_ready, 1)
                dve.wait_ge(mixed_ready, b + 1)
                for t in range(TILES):
                    last = nc.vector.bn_stats(stats[:, t, :], mixed[:, t, :])
                last.then_inc(stats_ready, 1)
                dve.wait_ge(stats_ready, b + 1)
                even_mean, even_dev = stats[:, :, 1], stats[:, :, 2]
                odd_mean, odd_dev = stats[:, :, 4], stats[:, :, 5]
                nc.vector.tensor_tensor(mean_sum[:, :], even_mean, odd_mean, ALU.add)
                nc.vector.tensor_tensor(mean_gap[:, :], even_mean, odd_mean, ALU.subtract)
                nc.vector.tensor_tensor(deviation[:, :], even_dev, odd_dev, ALU.add)\
                  .then_inc(merge_step, 1)
                dve.wait_ge(merge_step, 2 * b + 1)
                nc.vector.scalar_tensor_tensor(square_gap[:, :], mean_gap[:, :], 0.25,
                                               mean_gap[:, :], ALU.mult, ALU.mult)\
                  .then_inc(merge_step, 1)
                dve.wait_ge(merge_step, 2 * b + 2)
                nc.vector.scalar_tensor_tensor(variance[:, :], deviation[:, :], 1.0 / D,
                                               square_gap[:, :], ALU.mult, ALU.add)\
                  .then_inc(variance_ready, 1)

            def invert(b):
                def step(instruction, n):
                    instruction.then_inc(rstd_step, 1)
                    dve.wait_ge(rstd_step, RSTD_STEPS * b + n)

                RSTD_STEPS = 5
                dve.wait_ge(std_ready, b + 1)
                nc.vector.tensor_scalar(var_eps[:, :], variance[:, :], EPS, None, ALU.add)
                step(nc.vector.reciprocal(guess[:, :], std[:, :]), 1)
                step(nc.vector.tensor_tensor(square[:, :], guess[:, :], guess[:, :], ALU.mult), 2)
                step(nc.vector.tensor_tensor(factor[:, :], square[:, :], var_eps[:, :],
                                             ALU.mult), 3)
                step(nc.vector.tensor_scalar(factor[:, :], factor[:, :], -0.5, 1.5,
                                             ALU.mult, ALU.add), 4)
                step(nc.vector.tensor_tensor(rstd[:, :], guess[:, :], factor[:, :], ALU.mult), 5)
                nc.vector.scalar_tensor_tensor(shift[:, :], mean_sum[:, :], -0.5, rstd[:, :],
                                               ALU.mult, ALU.mult).then_inc(rstd_ready, 1)

            nc.vector.memset(eps[:, :], EPS).then_inc(eps_ready, 1)
            dve.wait_ge(gate_ready, 1)
            nc.vector.tensor_scalar(keep[:, :, :], gate[:, :, :], -1.0, 2.0, ALU.mult, ALU.add)\
              .then_inc(keep_ready, 1)
            for r in range(ROUNDS):
                for s in range(RING):
                    if r * RING + s in X_SPLIT_AT:
                        split_x_low(X_SPLIT_AT.index(r * RING + s))
                    split_low(r, s)
            dve.wait_ge(keep_ready, 1)

            def stream_block(b, first_block):
                r0 = b * ROUNDS
                stream(r0, r0 + 4)
                mix(b - 1, first_block)
                stream(r0 + 4, r0 + 6)
                invert(b - 1)
                stream(r0 + 6, r0 + 8)

            stream_block(1, True)
            with dve.Fori(2, BLOCKS) as b:
                stream_block(b, False)
            mix(BLOCKS - 1, False)
            invert(BLOCKS - 1)

        @block.tensor
        def _(pe):
            def second_product(b, first_block):
                pe.wait_ge(y_copied, b + 1)
                if not first_block:
                    pe.wait_ge(gated_ready, b)
                for t in range(TILES):
                    last = nc.tensor.matmul(agg[:, t, :], y_t[:, t, :], weights[:, :],
                                            start=True, stop=True)
                last.then_inc(agg_ready, 1)

            def stream_block(b, parity, position):
                for g in range(GROUPS):
                    slot = g % RING
                    if b is FIRST and g % (GROUPS // X_PIECES) == 0:
                        pe.wait_ge(x_high_ready, g // (GROUPS // X_PIECES) + 1)
                        pe.wait_ge(x_low_ready, g // (GROUPS // X_PIECES) + 1)
                    pe.wait_ge(low_ready, GROUPS * b + g + 1)
                    if g == 0 and position >= 2:
                        pe.wait_ge(y_copied, b - 1)
                    for c in range(GROUP_CHUNKS):
                        chunk = g * GROUP_CHUNKS + c
                        for x_part, adj_part in ((x_high, adj_high), (x_high, adj_low),
                                                 (x_low, adj_high)):
                            for h in range(HALVES):
                                at = c * BLOCK + h * BANK
                                last = nc.tensor.matmul(
                                    y_acc[:, parity, h, :],
                                    x_part[:, chunk * D:(chunk + 1) * D],
                                    adj_part[:, slot, at:at + BANK],
                                    start=(chunk == 0 and x_part is x_high
                                           and adj_part is adj_high),
                                    stop=(chunk == CHUNKS - 1 and x_part is x_low))
                    last.then_inc(group_used, 1)
                    if g == 2 * RING - 1 and position >= 1:
                        second_product(b - 1, position == 1)

            FIRST = 0
            pe.wait_ge(weights_landed, 16)
            stream_block(FIRST, 0, 0)
            stream_block(1, 1, 1)
            with pe.Fori(1, BLOCKS // 2) as pair:
                stream_block(2 * pair, 0, 2)
                stream_block(2 * pair + 1, 1, 2)
            second_product(BLOCKS - 1, False)


def kernel(x, adj, L0_gnn_w, L0_gnn_W_agg):
    import concourse.bacc as bacc
    import numpy as np
    from concourse.bass_utils import run_bass_kernel_spmd

    adj_groups = np.ascontiguousarray(
        np.asarray(adj).reshape(BLOCKS, P, TILES, P, GROUPS, GROUP_CHUNKS)
        .transpose(0, 4, 3, 5, 2, 1)).reshape(BLOCKS * GROUPS, P, GROUP)
    arrays = {
        "adj_groups": adj_groups,
        "x_chunks": np.ascontiguousarray(x).reshape(P, CHUNKS * D),
        "x_rows": np.ascontiguousarray(x).reshape(BLOCKS, P, TILES, D),
        "gate_w": np.ascontiguousarray(
            np.asarray(L0_gnn_w).reshape(BLOCKS, P, TILES).transpose(1, 0, 2)),
        "w_agg": np.ascontiguousarray(L0_gnn_W_agg),
    }
    nc = bacc.Bacc("TRN2", target_bir_lowering=False, num_devices=1)
    ins = [nc.dram_tensor(name, a.shape, mybir.dt.from_np(a.dtype), kind="ExternalInput").ap()
           for name, a in arrays.items()]
    out = nc.dram_tensor("out_rows", (BLOCKS, P, TILES, D), F32, kind="ExternalOutput").ap()
    build(nc, *ins, out)
    result = run_bass_kernel_spmd(nc, [arrays], core_ids=[0])
    return result.results[0]["out_rows"].reshape(NODES, D)
```

```python
from contextlib import ExitStack

import concourse.bass as bass
from concourse import mybir

F32 = mybir.dt.float32
F32R = mybir.dt.float32r
ALU = mybir.AluOpType
ACT = mybir.ActivationFunctionType

P = 128
NODES = 8192
D = 128
EPS = 1e-5

BLOCK = 1024
BLOCKS = NODES // BLOCK
TILES = BLOCK // P
BANK = 512
HALVES = BLOCK // BANK
HALF_TILES = TILES // HALVES
assert HALVES == 2 and BLOCKS % 2 == 0

CHUNKS = NODES // P
GROUP_CHUNKS = 2
GROUP = GROUP_CHUNKS * BLOCK
GROUPS = CHUNKS // GROUP_CHUNKS
RING = 4
ROUNDS = GROUPS // RING
ROUND_CHUNKS = RING * GROUP_CHUNKS

X_LOADS = [(0, 8, 0), (8, 16, 1), (16, 32, 3), (32, 48, 6), (48, 64, 12)]
X_SPLITS = [(0, 2, 0), (2, 8, 1), (8, 16, 3), (16, 32, 6), (32, 48, 12), (48, 64, 20)]


def load_of(chunk_end):
    return next(n for n, (_, end, _) in enumerate(X_LOADS) if end >= chunk_end)


def build(nc, adj_groups, x_rows, gate_w, w_agg, out_rows):
    with ExitStack() as ctx:
        def sbuf(name, shape, dtype=F32):
            return ctx.enter_context(nc.sbuf_tensor(name, shape, dtype))

        def psum(name, shape):
            return ctx.enter_context(nc.psum_tensor(name, shape, F32))

        def semaphore(name):
            return ctx.enter_context(nc.semaphore(name))

        adj_raw = sbuf("adj_raw", [P, RING, GROUP])
        adj_high = sbuf("adj_high", [P, RING, GROUP], F32R)
        adj_low = sbuf("adj_low", [P, RING, GROUP], F32R)
        x_all = sbuf("x_all", [P, CHUNKS, D])
        x_high = sbuf("x_high", [P, CHUNKS, D], F32R)
        x_low = sbuf("x_low", [P, CHUNKS, D], F32R)
        weights = sbuf("weights", [D, D])
        gate_logits = sbuf("gate_logits", [P, BLOCKS, TILES])
        gate = sbuf("gate", [P, BLOCKS, TILES])
        keep = sbuf("keep", [P, BLOCKS, TILES])
        y_t = sbuf("y_t", [D, TILES, P])
        rows = sbuf("rows", [P, TILES, D])
        stats = sbuf("stats", [P, TILES, 6])
        mean_sum = sbuf("mean_sum", [P, TILES])
        mean_gap = sbuf("mean_gap", [P, TILES])
        square_gap = sbuf("square_gap", [P, TILES])
        deviation = sbuf("deviation", [P, TILES])
        variance = sbuf("variance", [P, TILES])
        eps = sbuf("eps", [P, 1])
        std = sbuf("std", [P, TILES])
        var_eps = sbuf("var_eps", [P, TILES])
        guess = sbuf("guess", [P, TILES])
        square = sbuf("square", [P, TILES])
        product = sbuf("product", [P, TILES])
        factor = sbuf("factor", [P, TILES])
        rstd = sbuf("rstd", [P, TILES])
        shift = sbuf("shift", [P, TILES])

        y_acc = psum("y_acc", [D, 2, HALVES, BANK])
        agg = psum("agg", [P, TILES, D])

        adj_landed = [semaphore(f"adj_landed{s}") for s in range(RING)]
        first_chunk_landed = semaphore("first_chunk_landed")
        last_chunk_landed = semaphore("last_chunk_landed")
        x_landed = [semaphore(f"x_landed{n}") for n in range(len(X_LOADS))]
        weights_landed = semaphore("weights_landed")
        logits_landed = semaphore("logits_landed")
        out_stored = semaphore("out_stored")
        x_high_ready = semaphore("x_high_ready")
        x_low_ready = semaphore("x_low_ready")
        high_ready = semaphore("high_ready")
        low_ready = semaphore("low_ready")
        group_used = semaphore("group_used")
        first_half_summed = semaphore("first_half_summed")
        y_copied = semaphore("y_copied")
        agg_ready = semaphore("agg_ready")
        gated_ready = semaphore("gated_ready")
        mixed_ready = semaphore("mixed_ready")
        stats_ready = semaphore("stats_ready")
        variance_ready = semaphore("variance_ready")
        std_ready = semaphore("std_ready")
        rstd_ready = semaphore("rstd_ready")
        normed_ready = semaphore("normed_ready")
        last_y_copied = semaphore("last_y_copied")
        last_normed_ready = semaphore("last_normed_ready")
        merge_step = semaphore("merge_step")
        invert_step = semaphore("invert_step")
        gate_ready = semaphore("gate_ready")
        keep_ready = semaphore("keep_ready")
        eps_ready = semaphore("eps_ready")

        block = ctx.enter_context(nc.Block())

        LAST = BLOCKS - 1

        def halves_done(b, half, halves):
            return HALVES * b + half + halves

        def tiles_of(half, halves):
            return slice(half * HALF_TILES, (half + halves) * HALF_TILES)

        @block.sync
        def _(sp):
            def free_slot(round_, slot):
                sp.wait_ge(low_ready, ROUND_CHUNKS * (round_ - 1) + GROUP_CHUNKS * (slot + 1))

            def load_group(round_, slot):
                sp.dma_start(adj_raw[:, slot, :], adj_groups[round_ * RING + slot])\
                  .then_inc(adj_landed[slot], 16)

            def load_halves(group, slot, first_landed):
                sp.dma_start(adj_raw[:, slot, 0:BLOCK], adj_groups[group, :, 0:BLOCK])\
                  .then_inc(first_landed, 16)
                sp.dma_start(adj_raw[:, slot, BLOCK:GROUP], adj_groups[group, :, BLOCK:GROUP])\
                  .then_inc(adj_landed[slot], 16)

            for r in range(ROUNDS):
                for s in range(RING):
                    for n, (c0, c1, ahead_of) in enumerate(X_LOADS):
                        if ahead_of == r * RING + s:
                            b0, b1 = c0 // TILES, c1 // TILES
                            sp.dma_start(
                                x_all[:, c0:c1, :].rearrange("p (b t) d -> p b (t d)", t=TILES),
                                x_rows[b0:b1].rearrange("b p n -> p b n"))\
                              .then_inc(x_landed[n], 16)
                    if r > 0:
                        free_slot(r, s)
                        load_group(r, s)
                    elif s > 0:
                        load_group(r, s)
                    else:
                        load_halves(0, 0, first_chunk_landed)
            end = BLOCKS * ROUNDS - 1
            with sp.Fori(ROUNDS, end) as r:
                for s in range(RING):
                    free_slot(r, s)
                    load_group(r, s)
            for s in range(RING - 1):
                free_slot(end, s)
                load_group(end, s)
            free_slot(end, RING - 1)
            load_halves(BLOCKS * GROUPS - 1, RING - 1, last_chunk_landed)

            for half, ready, count in ((0, normed_ready, halves_done(LAST, 0, 1)),
                                       (1, last_normed_ready, 1)):
                t = tiles_of(half, 1)
                sp.wait_ge(ready, count)
                sp.dma_start(out_rows[LAST, :, t, :], rows[:, t, :]).then_inc(out_stored, 16)
            sp.wait_ge(out_stored, 16 * (LAST + HALVES))

        @block.scalar
        def _(act):
            def raw_landed(round_, slot):
                act.wait_ge(adj_landed[slot], 16 * (round_ + 1))

            def parts_free(round_, slot):
                act.wait_ge(group_used, RING * (round_ - 1) + slot + 1)

            def split_high(slot, first, end):
                part = slice(first * BLOCK, end * BLOCK)
                nc.scalar.activation(adj_high[:, slot, part], adj_raw[:, slot, part], ACT.Copy)\
                  .then_inc(high_ready, end - first)

            def split_group(round_, slot, first_round):
                raw_landed(round_, slot)
                if not first_round:
                    parts_free(round_, slot)
                split_high(slot, 0, GROUP_CHUNKS)

            def split_x_high(n):
                c0, c1, _ = X_SPLITS[n]
                act.wait_ge(x_landed[load_of(c1)], 16)
                nc.scalar.activation(x_high[:, c0:c1, :], x_all[:, c0:c1, :], ACT.Copy)\
                  .then_inc(x_high_ready, 1)

            def stream(first, end):
                with act.Fori(first, end) as r:
                    for s in range(RING):
                        split_group(r, s, False)

            def copy_y(b, parity, half, halves):
                if half + halves == HALVES:
                    act.wait_ge(group_used, GROUPS * (b + 1))
                else:
                    act.wait_ge(first_half_summed, b + 1)
                nc.scalar.activation(
                    y_t[:, tiles_of(half, halves), :].rearrange("d t p -> d (t p)"),
                    y_acc[:, parity, half:half + halves, :].rearrange("d h n -> d (h n)"),
                    ACT.Copy).then_inc(y_copied, halves)

            def gate_agg(b, half, halves, first_block):
                act.wait_ge(agg_ready, halves_done(b, half, halves))
                if not first_block:
                    act.wait_ge(out_stored, 16 * b)
                for t in range(half * HALF_TILES, (half + halves) * HALF_TILES):
                    last = nc.scalar.activation(rows[:, t, :], agg[:, t, :], ACT.Relu,
                                                scale=gate[:, b, t:t + 1])
                last.then_inc(gated_ready, halves)

            def root(b, half, halves):
                act.wait_ge(variance_ready, halves_done(b, half, halves))
                t = tiles_of(half, halves)
                nc.scalar.activation(std[:, t], variance[:, t], ACT.Sqrt, bias=eps[:, 0:1])\
                  .then_inc(std_ready, halves)

            def normalize(b, half, halves):
                act.wait_ge(rstd_ready, halves_done(b, half, halves))
                for t in range(half * HALF_TILES, (half + halves) * HALF_TILES):
                    last = nc.scalar.activation(rows[:, t, :], rows[:, t, :], ACT.Identity,
                                                scale=rstd[:, t:t + 1], bias=shift[:, t:t + 1])
                last.then_inc(normed_ready, halves)

            def store(b):
                act.wait_ge(normed_ready, halves_done(b, 0, HALVES))
                act.dma_start(out_rows[b], rows[:, :, :]).then_inc(out_stored, 16)

            def stream_block(b, parity_before, first_block):
                r0 = b * ROUNDS
                stream(r0, r0 + 1)
                copy_y(b - 1, parity_before, 0, HALVES)
                stream(r0 + 1, r0 + 3)
                gate_agg(b - 1, 0, HALVES, first_block)
                stream(r0 + 3, r0 + 5)
                root(b - 1, 0, HALVES)
                stream(r0 + 5, r0 + 6)
                normalize(b - 1, 0, HALVES)
                stream(r0 + 6, r0 + 7)
                store(b - 1)

            act.dma_start(gate_logits[:, :, :], gate_w).then_inc(logits_landed, 16)
            act.dma_start(weights[:, :], w_agg).then_inc(weights_landed, 16)
            for r in range(ROUNDS):
                for s in range(RING):
                    for n, (_, _, ahead_of) in enumerate(X_SPLITS):
                        if ahead_of == r * RING + s:
                            split_x_high(n)
                    if r == 0 and s == 0:
                        act.wait_ge(first_chunk_landed, 16)
                        split_high(0, 0, 1)
                        raw_landed(0, 0)
                        split_high(0, 1, GROUP_CHUNKS)
                    else:
                        split_group(r, s, r == 0)
                if r == 0:
                    act.wait_ge(logits_landed, 16)
                    nc.scalar.activation(gate[:, :, :], gate_logits[:, :, :], ACT.Sigmoid)\
                      .then_inc(gate_ready, 1)
            act.wait_ge(eps_ready, 1)
            act.wait_ge(gate_ready, 1)

            stream_block(1, 0, True)
            stream(2 * ROUNDS - 1, 2 * ROUNDS)
            with act.Fori(1, BLOCKS // 2 - 1) as pair:
                for odd in range(2):
                    b = 2 * pair + odd
                    stream_block(b, 1 - odd, False)
                    stream(b * ROUNDS + ROUNDS - 1, b * ROUNDS + ROUNDS)
            stream_block(LAST - 1, 1, False)
            stream(LAST * ROUNDS - 1, LAST * ROUNDS)
            stream_block(LAST, 0, False)
            end = BLOCKS * ROUNDS - 1
            for s in range(RING - 1):
                split_group(end, s, False)
            act.wait_ge(last_chunk_landed, 16)
            parts_free(end, RING - 1)
            split_high(RING - 1, 0, 1)
            raw_landed(end, RING - 1)
            split_high(RING - 1, 1, GROUP_CHUNKS)

            copy_y(LAST, 1, 0, 1)
            gate_agg(LAST, 0, 1, False)
            gate_agg(LAST, 1, 1, False)
            root(LAST, 0, 1)
            root(LAST, 1, 1)
            normalize(LAST, 0, 1)

        @block.vector
        def _(dve):
            def split_low(chunk_count, slot, first, end):
                dve.wait_ge(high_ready, chunk_count)
                part = slice(first * BLOCK, end * BLOCK)
                nc.vector.tensor_tensor(adj_low[:, slot, part], adj_raw[:, slot, part],
                                        adj_high[:, slot, part].bitcast(F32), ALU.subtract)\
                  .then_inc(low_ready, end - first)

            def split_group(round_, slot):
                split_low(ROUND_CHUNKS * round_ + GROUP_CHUNKS * (slot + 1), slot,
                          0, GROUP_CHUNKS)

            def split_halves(group, slot):
                split_low(GROUP_CHUNKS * group + 1, slot, 0, 1)
                split_low(GROUP_CHUNKS * group + 2, slot, 1, 2)

            def split_x_low(n):
                c0, c1, _ = X_SPLITS[n]
                dve.wait_ge(x_high_ready, n + 1)
                nc.vector.tensor_tensor(x_low[:, c0:c1, :], x_all[:, c0:c1, :],
                                        x_high[:, c0:c1, :].bitcast(F32), ALU.subtract)\
                  .then_inc(x_low_ready, 1)

            def stream(first, end):
                with dve.Fori(first, end) as r:
                    for s in range(RING):
                        split_group(r, s)

            def mix(b, half, halves):
                dve.wait_ge(gated_ready, halves_done(b, half, halves))
                for t in range(half * HALF_TILES, (half + halves) * HALF_TILES):
                    last = nc.vector.scalar_tensor_tensor(
                        rows[:, t, :], x_all[:, b * TILES + t, :], keep[:, b, t:t + 1],
                        rows[:, t, :], ALU.mult, ALU.add)
                last.then_inc(mixed_ready, halves)
                dve.wait_ge(mixed_ready, halves_done(b, half, halves))
                for t in range(half * HALF_TILES, (half + halves) * HALF_TILES):
                    last = nc.vector.bn_stats(stats[:, t, :], rows[:, t, :])
                last.then_inc(stats_ready, halves)
                dve.wait_ge(stats_ready, halves_done(b, half, halves))
                ts = tiles_of(half, halves)
                even_mean, even_dev = stats[:, ts, 1], stats[:, ts, 2]
                odd_mean, odd_dev = stats[:, ts, 4], stats[:, ts, 5]
                MERGE_STEPS = 2
                done = MERGE_STEPS * halves_done(b, half, 0)
                nc.vector.tensor_tensor(mean_gap[:, ts], even_mean, odd_mean, ALU.subtract)
                nc.vector.tensor_tensor(mean_sum[:, ts], even_mean, odd_mean, ALU.add)
                nc.vector.tensor_tensor(deviation[:, ts], even_dev, odd_dev, ALU.add)\
                  .then_inc(merge_step, halves)
                dve.wait_ge(merge_step, done + halves)
                nc.vector.scalar_tensor_tensor(square_gap[:, ts], mean_gap[:, ts], 0.25,
                                               mean_gap[:, ts], ALU.mult, ALU.mult)\
                  .then_inc(merge_step, halves)
                dve.wait_ge(merge_step, done + 2 * halves)
                nc.vector.scalar_tensor_tensor(variance[:, ts], deviation[:, ts], 1.0 / D,
                                               square_gap[:, ts], ALU.mult, ALU.add)\
                  .then_inc(variance_ready, halves)

            def invert(b, half, halves):
                ts = tiles_of(half, halves)
                INVERT_STEPS = 5
                done = INVERT_STEPS * halves_done(b, half, 0)
                dve.wait_ge(std_ready, halves_done(b, half, halves))
                nc.vector.tensor_scalar(var_eps[:, ts], variance[:, ts], EPS, None, ALU.add)
                nc.vector.reciprocal(guess[:, ts], std[:, ts]).then_inc(invert_step, halves)
                dve.wait_ge(invert_step, done + halves)
                nc.vector.tensor_tensor(square[:, ts], guess[:, ts], guess[:, ts], ALU.mult)\
                  .then_inc(invert_step, halves)
                dve.wait_ge(invert_step, done + 2 * halves)
                nc.vector.tensor_tensor(product[:, ts], square[:, ts], var_eps[:, ts], ALU.mult)\
                  .then_inc(invert_step, halves)
                dve.wait_ge(invert_step, done + 3 * halves)
                nc.vector.tensor_scalar(factor[:, ts], product[:, ts], -0.5, 1.5,
                                        ALU.mult, ALU.add).then_inc(invert_step, halves)
                dve.wait_ge(invert_step, done + 4 * halves)
                nc.vector.tensor_tensor(rstd[:, ts], guess[:, ts], factor[:, ts], ALU.mult)\
                  .then_inc(invert_step, halves)
                dve.wait_ge(invert_step, done + 5 * halves)
                nc.vector.scalar_tensor_tensor(shift[:, ts], mean_sum[:, ts], -0.5, rstd[:, ts],
                                               ALU.mult, ALU.mult).then_inc(rstd_ready, halves)

            def stream_block(b):
                r0 = b * ROUNDS
                stream(r0, r0 + 3)
                mix(b - 1, 0, 1)
                stream(r0 + 3, r0 + 4)
                mix(b - 1, 1, 1)
                stream(r0 + 4, r0 + 5)
                invert(b - 1, 0, HALVES)
                stream(r0 + 5, r0 + 7)

            nc.vector.memset(eps[:, :], EPS).then_inc(eps_ready, 1)
            for r in range(ROUNDS):
                for s in range(RING):
                    for n, (_, _, ahead_of) in enumerate(X_SPLITS):
                        if ahead_of == r * RING + s:
                            split_x_low(n)
                    if r == 0 and s == 0:
                        split_halves(0, 0)
                    else:
                        split_group(r, s)
                if r == 1:
                    dve.wait_ge(gate_ready, 1)
                    nc.vector.tensor_scalar(keep[:, :, :], gate[:, :, :], -1.0, 2.0,
                                            ALU.mult, ALU.add).then_inc(keep_ready, 1)
            dve.wait_ge(keep_ready, 1)
            with dve.Fori(1, LAST) as b:
                stream_block(b)
                stream(b * ROUNDS + ROUNDS - 1, b * ROUNDS + ROUNDS)
            stream_block(LAST)
            end = BLOCKS * ROUNDS - 1
            for s in range(RING - 1):
                split_group(end, s)
            split_halves(BLOCKS * GROUPS - 1, RING - 1)

            dve.wait_ge(group_used, GROUPS * BLOCKS)
            nc.vector.tensor_copy(y_t[:, tiles_of(1, 1), :].rearrange("d t p -> d (t p)"),
                                  y_acc[:, LAST % 2, 1, :]).then_inc(last_y_copied, 1)
            mix(LAST, 0, 1)
            mix(LAST, 1, 1)
            invert(LAST, 0, 1)
            invert(LAST, 1, 1)
            dve.wait_ge(rstd_ready, halves_done(LAST, 1, 1))
            for t in range(HALF_TILES, TILES):
                last = nc.vector.tensor_scalar(rows[:, t, :], rows[:, t, :], rstd[:, t:t + 1],
                                               shift[:, t:t + 1], ALU.mult, ALU.add)
            last.then_inc(last_normed_ready, 1)

        @block.tensor
        def _(pe):
            def second_product(half, halves):
                for t in range(half * HALF_TILES, (half + halves) * HALF_TILES):
                    last = nc.tensor.matmul(agg[:, t, :], y_t[:, t, :], weights[:, :],
                                            start=True, stop=True)
                last.then_inc(agg_ready, halves)

            def products(chunk):
                parts = ((x_high, adj_high), (x_high, adj_low), (x_low, adj_high))
                if chunk < CHUNKS - 1:
                    return [(x, a, h) for x, a in parts for h in range(HALVES)]
                return [(x, a, h) for h in range(HALVES) for x, a in parts]

            def stream_block(b, parity, before):
                for chunk in range(CHUNKS):
                    g, c = divmod(chunk, GROUP_CHUNKS)
                    if before == 0:
                        for n, (first, _, _) in enumerate(X_SPLITS):
                            if first == chunk:
                                pe.wait_ge(x_low_ready, n + 1)
                    pe.wait_ge(low_ready, CHUNKS * b + chunk + 1)
                    if chunk == 0 and before >= 2:
                        pe.wait_ge(y_copied, halves_done(b - 2, 0, HALVES))
                    for x_part, adj_part, h in products(chunk):
                        at = c * BLOCK + h * BANK
                        ends = x_part is x_low
                        last = nc.tensor.matmul(
                            y_acc[:, parity, h, :], x_part[:, chunk, :],
                            adj_part[:, g % RING, at:at + BANK],
                            start=(chunk == 0 and x_part is x_high and adj_part is adj_high),
                            stop=(chunk == CHUNKS - 1 and ends))
                        if chunk == CHUNKS - 1 and ends and h == 0:
                            last.then_inc(first_half_summed, 1)
                    if c == GROUP_CHUNKS - 1:
                        last.then_inc(group_used, 1)
                    if chunk == 2 * ROUND_CHUNKS - 1 and before >= 1:
                        pe.wait_ge(y_copied, halves_done(b - 1, 0, HALVES))
                        if before >= 2:
                            pe.wait_ge(gated_ready, halves_done(b - 2, 0, HALVES))
                        second_product(0, HALVES)

            stream_block(0, 0, 0)
            pe.wait_ge(weights_landed, 16)
            stream_block(1, 1, 1)
            with pe.Fori(1, BLOCKS // 2) as pair:
                stream_block(2 * pair, 0, 2)
                stream_block(2 * pair + 1, 1, 2)
            pe.wait_ge(gated_ready, halves_done(LAST - 1, 0, HALVES))
            pe.wait_ge(y_copied, halves_done(LAST, 0, 1))
            second_product(0, 1)
            pe.wait_ge(last_y_copied, 1)
            second_product(1, 1)


def kernel(x, adj, L0_gnn_w, L0_gnn_W_agg):
    import concourse.bacc as bacc
    import numpy as np
    from concourse.bass_utils import run_bass_kernel_spmd

    adj_groups = np.ascontiguousarray(
        np.asarray(adj)
        .reshape(BLOCKS, P, TILES, BLOCKS, P, TILES // GROUP_CHUNKS, GROUP_CHUNKS)
        .transpose(0, 3, 5, 4, 6, 2, 1)).reshape(BLOCKS * GROUPS, P, GROUP)
    arrays = {
        "adj_groups": adj_groups,
        "x_rows": np.ascontiguousarray(x).reshape(BLOCKS, P, TILES * D),
        "gate_w": np.ascontiguousarray(
            np.asarray(L0_gnn_w).reshape(BLOCKS, P, TILES).transpose(1, 0, 2)),
        "w_agg": np.ascontiguousarray(L0_gnn_W_agg),
    }
    nc = bacc.Bacc("TRN2", target_bir_lowering=False, num_devices=1)
    ins = [nc.dram_tensor(name, a.shape, mybir.dt.from_np(a.dtype), kind="ExternalInput").ap()
           for name, a in arrays.items()]
    out = nc.dram_tensor("out_rows", (BLOCKS, P, TILES, D), F32, kind="ExternalOutput").ap()
    build(nc, *ins, out)
    result = run_bass_kernel_spmd(nc, [arrays], core_ids=[0])
    return result.results[0]["out_rows"].reshape(NODES, D)
```

```python
from contextlib import ExitStack

import concourse.bass as bass
from concourse import mybir

F32 = mybir.dt.float32
F32R = mybir.dt.float32r
ALU = mybir.AluOpType
ACT = mybir.ActivationFunctionType

P = 128
NODES = 8192
D = 128
EPS = 1e-5

BLOCK = 512
BLOCKS = NODES // BLOCK
LAST = BLOCKS - 1
TILES = BLOCK // P

CHUNKS = NODES // P
GROUP_CHUNKS = 4
GROUP = GROUP_CHUNKS * BLOCK
GROUPS = CHUNKS // GROUP_CHUNKS
RING = 4
ROUNDS = GROUPS // RING
ROUND_CHUNKS = RING * GROUP_CHUNKS
EDGE = 2
assert BLOCKS % 2 == 0 and GROUPS % RING == 0

X_LOADS = [(0, 8, 0), (8, 16, 1), (16, 32, 3), (32, 48, 6), (48, 64, 9)]
X_SPLITS = [(0, 2, 0), (2, 8, 1), (8, 16, 2), (16, 32, 3), (32, 48, 6), (48, 64, 10)]

COPY_AT = RING
PRODUCT_AT = RING
GATE_AT = 2 * RING
MIX_AT = 2 * RING + 1
STATS_AT = 2 * RING + 2
ROOT_AT = 3 * RING
INVERT_AT = 3 * RING + 1
NORMALIZE_AT = 3 * RING + 2
STORE_AT = 3 * RING + 3


def load_of(chunk_end):
    return next(n for n, (_, end, _) in enumerate(X_LOADS) if end >= chunk_end)


def pieces_ahead_of(group, pieces):
    return [n for n, (_, _, ahead_of) in enumerate(pieces) if ahead_of == group]


def build(nc, adj_groups, x_rows, gate_w, w_agg, out_rows):
    with ExitStack() as ctx:
        def sbuf(name, shape, dtype=F32):
            return ctx.enter_context(nc.sbuf_tensor(name, shape, dtype))

        def psum(name, shape):
            return ctx.enter_context(nc.psum_tensor(name, shape, F32))

        def semaphore(name):
            return ctx.enter_context(nc.semaphore(name))

        adj_raw = sbuf("adj_raw", [P, RING, GROUP])
        adj_high = sbuf("adj_high", [P, RING, GROUP], F32R)
        adj_low = sbuf("adj_low", [P, RING, GROUP], F32R)
        x_all = sbuf("x_all", [P, CHUNKS, D])
        x_high = sbuf("x_high", [P, CHUNKS, D], F32R)
        x_low = sbuf("x_low", [P, CHUNKS, D], F32R)
        weights = sbuf("weights", [D, D])
        gate_logits = sbuf("gate_logits", [P, BLOCKS, TILES])
        gate = sbuf("gate", [P, BLOCKS, TILES])
        keep = sbuf("keep", [P, BLOCKS, TILES])
        y_t = sbuf("y_t", [D, TILES, P])
        rows = sbuf("rows", [P, TILES, D])
        stats = sbuf("stats", [P, TILES, 6])
        mean_sum = sbuf("mean_sum", [P, TILES])
        mean_gap = sbuf("mean_gap", [P, TILES])
        square_gap = sbuf("square_gap", [P, TILES])
        deviation = sbuf("deviation", [P, TILES])
        variance = sbuf("variance", [P, TILES])
        eps = sbuf("eps", [P, 1])
        std = sbuf("std", [P, TILES])
        var_eps = sbuf("var_eps", [P, TILES])
        guess = sbuf("guess", [P, TILES])
        square = sbuf("square", [P, TILES])
        product = sbuf("product", [P, TILES])
        factor = sbuf("factor", [P, TILES])
        rstd = sbuf("rstd", [P, TILES])
        shift = sbuf("shift", [P, TILES])

        y_acc = psum("y_acc", [D, 2, BLOCK])
        agg = psum("agg", [P, TILES, BLOCK])

        adj_landed = [semaphore(f"adj_landed{s}") for s in range(RING)]
        first_piece_landed = semaphore("first_piece_landed")
        last_piece_landed = semaphore("last_piece_landed")
        x_landed = [semaphore(f"x_landed{n}") for n in range(len(X_LOADS))]
        weights_landed = semaphore("weights_landed")
        logits_landed = semaphore("logits_landed")
        out_stored = semaphore("out_stored")
        x_high_ready = semaphore("x_high_ready")
        x_low_ready = semaphore("x_low_ready")
        high_ready = semaphore("high_ready")
        low_ready = semaphore("low_ready")
        group_used = semaphore("group_used")
        y_copied = semaphore("y_copied")
        agg_ready = semaphore("agg_ready")
        gated_ready = semaphore("gated_ready")
        mixed_ready = semaphore("mixed_ready")
        stats_ready = semaphore("stats_ready")
        variance_ready = semaphore("variance_ready")
        std_ready = semaphore("std_ready")
        rstd_ready = semaphore("rstd_ready")
        normed_ready = semaphore("normed_ready")
        last_normed_ready = semaphore("last_normed_ready")
        merge_step = semaphore("merge_step")
        invert_step = semaphore("invert_step")
        gate_ready = semaphore("gate_ready")
        keep_ready = semaphore("keep_ready")
        eps_ready = semaphore("eps_ready")

        block = ctx.enter_context(nc.Block())

        @block.sync
        def _(sp):
            def free_slot(round_, slot):
                sp.wait_ge(low_ready, ROUND_CHUNKS * (round_ - 1) + GROUP_CHUNKS * (slot + 1))

            def load_group(round_, slot):
                sp.dma_start(adj_raw[:, slot, :], adj_groups[round_ * RING + slot])\
                  .then_inc(adj_landed[slot], 16)

            def load_pieces(group, slot, first_landed):
                cut = EDGE * BLOCK
                sp.dma_start(adj_raw[:, slot, 0:cut], adj_groups[group, :, 0:cut])\
                  .then_inc(first_landed, 16)
                sp.dma_start(adj_raw[:, slot, cut:GROUP], adj_groups[group, :, cut:GROUP])\
                  .then_inc(adj_landed[slot], 16)

            for g in range(GROUPS):
                for n in pieces_ahead_of(g, X_LOADS):
                    c0, c1, _ = X_LOADS[n]
                    sp.dma_start(
                        x_all[:, c0:c1, :].rearrange("p (b t) d -> p b (t d)", t=TILES),
                        x_rows[c0 // TILES:c1 // TILES].rearrange("b p n -> p b n"))\
                      .then_inc(x_landed[n], 16)
                if g == 0:
                    load_pieces(0, 0, first_piece_landed)
                    continue
                if g >= RING:
                    free_slot(g // RING, g % RING)
                load_group(g // RING, g % RING)
            end = BLOCKS * ROUNDS - 1
            with sp.Fori(ROUNDS, end) as r:
                for s in range(RING):
                    free_slot(r, s)
                    load_group(r, s)
            for s in range(RING - 1):
                free_slot(end, s)
                load_group(end, s)
            free_slot(end, RING - 1)
            load_pieces(BLOCKS * GROUPS - 1, RING - 1, last_piece_landed)

            sp.wait_ge(normed_ready, BLOCKS)
            sp.wait_ge(last_normed_ready, 1)
            sp.dma_start(out_rows[LAST], rows[:, :, :].rearrange("p t d -> p (t d)"))\
              .then_inc(out_stored, 16)
            sp.wait_ge(out_stored, 16 * BLOCKS)

        @block.scalar
        def _(act):
            def split_high(slot, first, end):
                part = slice(first * BLOCK, end * BLOCK)
                nc.scalar.activation(adj_high[:, slot, part], adj_raw[:, slot, part], ACT.Copy)\
                  .then_inc(high_ready, end - first)

            def split_group(b, g, has_before, in_pieces=False, lands=None):
                slot = g % RING
                round_ = b * ROUNDS + g // RING
                if lands is not None:
                    act.wait_ge(lands, 16)
                else:
                    act.wait_ge(adj_landed[slot], 16 * (round_ + 1))
                if has_before:
                    act.wait_ge(group_used, RING * (round_ - 1) + slot + 1)
                split_high(slot, 0, EDGE if in_pieces else GROUP_CHUNKS)
                if in_pieces:
                    if lands is not None:
                        act.wait_ge(adj_landed[slot], 16 * (round_ + 1))
                    split_high(slot, EDGE, GROUP_CHUNKS)

            def split_x_high(n):
                c0, c1, _ = X_SPLITS[n]
                act.wait_ge(x_landed[load_of(c1)], 16)
                nc.scalar.activation(x_high[:, c0:c1, :], x_all[:, c0:c1, :], ACT.Copy)\
                  .then_inc(x_high_ready, 1)

            def copy_y(b, parity, first, end):
                act.wait_ge(group_used, GROUPS * (b + 1))
                nc.scalar.activation(y_t[:, first:end, :].rearrange("d t p -> d (t p)"),
                                     y_acc[:, parity, first * P:end * P], ACT.Copy)\
                  .then_inc(y_copied, end - first)

            def gate_agg(b, first_block, tile_by_tile=False):
                if not first_block:
                    act.wait_ge(out_stored, 16 * b)
                if not tile_by_tile:
                    act.wait_ge(agg_ready, TILES * (b + 1))
                for t in range(TILES):
                    if tile_by_tile:
                        act.wait_ge(agg_ready, TILES * b + t + 1)
                    nc.scalar.activation(rows[:, t, :], agg[:, t, 0:D], ACT.Relu,
                                         scale=gate[:, b, t:t + 1]).then_inc(gated_ready, 1)

            def root(b):
                act.wait_ge(variance_ready, b + 1)
                nc.scalar.activation(std[:, :], variance[:, :], ACT.Sqrt, bias=eps[:, 0:1])\
                  .then_inc(std_ready, 1)

            def normalize(b, tiles):
                act.wait_ge(rstd_ready, b + 1)
                for t in range(tiles):
                    last = nc.scalar.activation(rows[:, t, :], rows[:, t, :], ACT.Identity,
                                                scale=rstd[:, t:t + 1], bias=shift[:, t:t + 1])
                last.then_inc(normed_ready, 1)

            def store(b):
                act.wait_ge(normed_ready, b + 1)
                act.dma_start(out_rows[b], rows[:, :, :].rearrange("p t d -> p (t d)"))\
                   .then_inc(out_stored, 16)

            def stream_block(b, parity, first_block=False, last_block=False):
                for g in range(GROUPS):
                    if g == COPY_AT:
                        copy_y(b - 1, 1 - parity, 0, TILES)
                    if g == GATE_AT:
                        gate_agg(b - 1, first_block)
                    if g == ROOT_AT:
                        root(b - 1)
                    if g == NORMALIZE_AT:
                        normalize(b - 1, TILES)
                    if g == STORE_AT:
                        store(b - 1)
                    ends = last_block and g >= GROUPS - RING
                    split_group(b, g, True, in_pieces=ends,
                                lands=last_piece_landed if ends and g == GROUPS - 1 else None)

            act.dma_start(gate_logits[:, :, :], gate_w).then_inc(logits_landed, 16)
            act.dma_start(weights[:, :], w_agg).then_inc(weights_landed, 16)
            for g in range(GROUPS):
                for n in pieces_ahead_of(g, X_SPLITS):
                    split_x_high(n)
                split_group(0, g, g >= RING, in_pieces=g == 0,
                            lands=first_piece_landed if g == 0 else None)
                if g == RING:
                    act.wait_ge(logits_landed, 16)
                    nc.scalar.activation(gate[:, :, :], gate_logits[:, :, :], ACT.Sigmoid)\
                      .then_inc(gate_ready, 1)
            act.wait_ge(eps_ready, 1)
            act.wait_ge(gate_ready, 1)

            stream_block(1, 1, first_block=True)
            with act.Fori(1, BLOCKS // 2 - 1) as pair:
                stream_block(2 * pair, 0)
                stream_block(2 * pair + 1, 1)
            stream_block(LAST - 1, 0)
            stream_block(LAST, 1, last_block=True)

            copy_y(LAST, 1, 0, TILES // 2)
            copy_y(LAST, 1, TILES // 2, TILES)
            gate_agg(LAST, False, tile_by_tile=True)
            root(LAST)
            normalize(LAST, TILES // 2)

        @block.vector
        def _(dve):
            def split_low(b, g, first, end):
                dve.wait_ge(high_ready, CHUNKS * b + GROUP_CHUNKS * g + end)
                slot = g % RING
                part = slice(first * BLOCK, end * BLOCK)
                nc.vector.tensor_tensor(adj_low[:, slot, part], adj_raw[:, slot, part],
                                        adj_high[:, slot, part].bitcast(F32), ALU.subtract)\
                  .then_inc(low_ready, end - first)

            def split_group(b, g, in_pieces=False):
                if in_pieces:
                    split_low(b, g, 0, EDGE)
                    split_low(b, g, EDGE, GROUP_CHUNKS)
                else:
                    split_low(b, g, 0, GROUP_CHUNKS)

            def split_x_low(n):
                c0, c1, _ = X_SPLITS[n]
                dve.wait_ge(x_high_ready, n + 1)
                nc.vector.tensor_tensor(x_low[:, c0:c1, :], x_all[:, c0:c1, :],
                                        x_high[:, c0:c1, :].bitcast(F32), ALU.subtract)\
                  .then_inc(x_low_ready, 1)

            def mix(b, tile_by_tile=False):
                if not tile_by_tile:
                    dve.wait_ge(gated_ready, TILES * (b + 1))
                for t in range(TILES):
                    if tile_by_tile:
                        dve.wait_ge(gated_ready, TILES * b + t + 1)
                    last = nc.vector.scalar_tensor_tensor(
                        rows[:, t, :], x_all[:, b * TILES + t, :], keep[:, b, t:t + 1],
                        rows[:, t, :], ALU.mult, ALU.add)
                last.then_inc(mixed_ready, 1)

            def moments(b):
                dve.wait_ge(mixed_ready, b + 1)
                for t in range(TILES):
                    last = nc.vector.bn_stats(stats[:, t, :], rows[:, t, :])
                last.then_inc(stats_ready, 1)
                dve.wait_ge(stats_ready, b + 1)
                even_mean, even_dev = stats[:, :, 1], stats[:, :, 2]
                odd_mean, odd_dev = stats[:, :, 4], stats[:, :, 5]
                MERGE_STEPS = 2
                nc.vector.tensor_tensor(mean_gap[:, :], even_mean, odd_mean, ALU.subtract)
                nc.vector.tensor_tensor(mean_sum[:, :], even_mean, odd_mean, ALU.add)
                nc.vector.tensor_tensor(deviation[:, :], even_dev, odd_dev, ALU.add)\
                  .then_inc(merge_step, 1)
                dve.wait_ge(merge_step, MERGE_STEPS * b + 1)
                nc.vector.scalar_tensor_tensor(square_gap[:, :], mean_gap[:, :], 0.25,
                                               mean_gap[:, :], ALU.mult, ALU.mult)\
                  .then_inc(merge_step, 1)
                dve.wait_ge(merge_step, MERGE_STEPS * b + 2)
                nc.vector.scalar_tensor_tensor(variance[:, :], deviation[:, :], 1.0 / D,
                                               square_gap[:, :], ALU.mult, ALU.add)\
                  .then_inc(variance_ready, 1)

            def invert(b):
                INVERT_STEPS = 5
                dve.wait_ge(std_ready, b + 1)
                nc.vector.tensor_scalar(var_eps[:, :], variance[:, :], EPS, None, ALU.add)
                nc.vector.reciprocal(guess[:, :], std[:, :]).then_inc(invert_step, 1)
                dve.wait_ge(invert_step, INVERT_STEPS * b + 1)
                nc.vector.tensor_tensor(square[:, :], guess[:, :], guess[:, :], ALU.mult)\
                  .then_inc(invert_step, 1)
                dve.wait_ge(invert_step, INVERT_STEPS * b + 2)
                nc.vector.tensor_tensor(product[:, :], square[:, :], var_eps[:, :], ALU.mult)\
                  .then_inc(invert_step, 1)
                dve.wait_ge(invert_step, INVERT_STEPS * b + 3)
                nc.vector.tensor_scalar(factor[:, :], product[:, :], -0.5, 1.5,
                                        ALU.mult, ALU.add).then_inc(invert_step, 1)
                dve.wait_ge(invert_step, INVERT_STEPS * b + 4)
                nc.vector.tensor_tensor(rstd[:, :], guess[:, :], factor[:, :], ALU.mult)\
                  .then_inc(invert_step, 1)
                dve.wait_ge(invert_step, INVERT_STEPS * b + 5)
                nc.vector.scalar_tensor_tensor(shift[:, :], mean_sum[:, :], -0.5, rstd[:, :],
                                               ALU.mult, ALU.mult).then_inc(rstd_ready, 1)

            def stream_block(b, last_block=False):
                for g in range(GROUPS):
                    if g == MIX_AT:
                        mix(b - 1)
                    if g == STATS_AT:
                        moments(b - 1)
                    if g == INVERT_AT:
                        invert(b - 1)
                    split_group(b, g, in_pieces=last_block and g >= GROUPS - RING)

            nc.vector.memset(eps[:, :], EPS).then_inc(eps_ready, 1)
            for g in range(GROUPS):
                for n in pieces_ahead_of(g, X_SPLITS):
                    split_x_low(n)
                split_group(0, g, in_pieces=g == 0)
            dve.wait_ge(gate_ready, 1)
            nc.vector.tensor_scalar(keep[:, :, :], gate[:, :, :], -1.0, 2.0,
                                    ALU.mult, ALU.add).then_inc(keep_ready, 1)
            dve.wait_ge(keep_ready, 1)
            with dve.Fori(1, LAST) as b:
                stream_block(b)
            stream_block(LAST, last_block=True)

            mix(LAST, tile_by_tile=True)
            moments(LAST)
            invert(LAST)
            dve.wait_ge(rstd_ready, BLOCKS)
            for t in range(TILES // 2, TILES):
                last = nc.vector.tensor_scalar(rows[:, t, :], rows[:, t, :], rstd[:, t:t + 1],
                                               shift[:, t:t + 1], ALU.mult, ALU.add)
            last.then_inc(last_normed_ready, 1)

        @block.tensor
        def _(pe):
            def second_product(first, end):
                for t in range(first, end):
                    nc.tensor.matmul(agg[:, t, 0:D], y_t[:, t, :], weights[:, :],
                                     start=True, stop=True).then_inc(agg_ready, 1)

            def stream_block(b, parity, before):
                for chunk in range(CHUNKS):
                    g, c = divmod(chunk, GROUP_CHUNKS)
                    if before == 0:
                        for n, (first, _, _) in enumerate(X_SPLITS):
                            if first == chunk:
                                pe.wait_ge(x_low_ready, n + 1)
                    if c % EDGE == 0:
                        pe.wait_ge(low_ready, CHUNKS * b + chunk + EDGE)
                    if chunk == 0 and before >= 2:
                        pe.wait_ge(y_copied, TILES * (b - 1))
                    if c == 0 and g == PRODUCT_AT and before >= 1:
                        pe.wait_ge(y_copied, TILES * b)
                        if before >= 2:
                            pe.wait_ge(gated_ready, TILES * (b - 1))
                        second_product(0, TILES)
                    part = slice(c * BLOCK, (c + 1) * BLOCK)
                    for n, (x_part, adj_part) in enumerate(
                            ((x_high, adj_high), (x_high, adj_low), (x_low, adj_high))):
                        last = nc.tensor.matmul(y_acc[:, parity, :], x_part[:, chunk, :],
                                                adj_part[:, g % RING, part],
                                                start=(chunk == 0 and n == 0),
                                                stop=(chunk == CHUNKS - 1 and n == 2))
                    if c == GROUP_CHUNKS - 1:
                        last.then_inc(group_used, 1)

            stream_block(0, 0, 0)
            pe.wait_ge(weights_landed, 16)
            stream_block(1, 1, 1)
            with pe.Fori(1, BLOCKS // 2) as pair:
                stream_block(2 * pair, 0, 2)
                stream_block(2 * pair + 1, 1, 2)
            pe.wait_ge(gated_ready, TILES * LAST)
            pe.wait_ge(y_copied, TILES * LAST + TILES // 2)
            second_product(0, TILES // 2)
            pe.wait_ge(y_copied, TILES * BLOCKS)
            second_product(TILES // 2, TILES)


def kernel(x, adj, L0_gnn_w, L0_gnn_W_agg):
    import concourse.bacc as bacc
    import numpy as np
    from concourse.bass_utils import run_bass_kernel_spmd

    assert TILES == GROUP_CHUNKS
    adj_groups = np.ascontiguousarray(
        np.asarray(adj).reshape(BLOCKS, P, TILES, GROUPS, P, GROUP_CHUNKS)
        .transpose(0, 3, 4, 5, 2, 1)).reshape(BLOCKS * GROUPS, P, GROUP)
    arrays = {
        "adj_groups": adj_groups,
        "x_rows": np.ascontiguousarray(x).reshape(BLOCKS, P, TILES * D),
        "gate_w": np.ascontiguousarray(
            np.asarray(L0_gnn_w).reshape(BLOCKS, P, TILES).transpose(1, 0, 2)),
        "w_agg": np.ascontiguousarray(L0_gnn_W_agg),
    }
    nc = bacc.Bacc("TRN2", target_bir_lowering=False, num_devices=1)
    ins = [nc.dram_tensor(name, a.shape, mybir.dt.from_np(a.dtype), kind="ExternalInput").ap()
           for name, a in arrays.items()]
    out = nc.dram_tensor("out_rows", (BLOCKS, P, TILES * D), F32, kind="ExternalOutput").ap()
    build(nc, *ins, out)
    result = run_bass_kernel_spmd(nc, [arrays], core_ids=[0])
    return result.results[0]["out_rows"].reshape(NODES, D)
```
